# Optimizing a Trainium2 kernel written in Bass

```python
import numpy as np
import jax
import jax.numpy as jnp

def _softmax(x, axis=-1):
    return jax.nn.softmax(x, axis=axis)

def _gelu(x):
    return jax.nn.gelu(x, approximate=True)

def _silu(x):
    return jax.nn.silu(x)

def _sigmoid(x):
    return jax.nn.sigmoid(x)

def _layernorm(x, axis=-1, eps=1e-05):
    m = jnp.mean(x, axis=axis, keepdims=True)
    v = jnp.var(x, axis=axis, keepdims=True)
    return (x - m) / jnp.sqrt(v + eps)

def _scatter_add(tgt, idx, src, axis=0):
    return tgt.at[idx].add(src)

def _segment_sum(src, seg, n):
    return jax.ops.segment_sum(src, seg, n)
kernel_name = 'mk_cond_resid_d2_seqx_r2_81a4c7'

def setup_inputs(seed: int=0):
    np.random.seed(seed)
    _w = jnp.asarray

    def _rec_inputs():
        import jax
        import jax.numpy as jnp
        _rk = jax.random.key(seed)
        x = -0.0003929 + 0.9999 * jax.random.normal(jax.random.fold_in(_rk, 1), (64, 128, 512), jnp.float32)
        _lenS = 128 - jax.random.randint(jax.random.fold_in(_rk, 7), (64,), 0, max(1, 128 // 4) + 1, jnp.int32)
        _lenS2 = 128 - jax.random.randint(jax.random.fold_in(_rk, 8), (64,), 0, max(1, 128 // 4) + 1, jnp.int32)
        itok_B_0_63 = jax.random.randint(jax.random.fold_in(_rk, 11), (64,), 0, 64, jnp.int32)
        itok_B_0_15 = jax.random.randint(jax.random.fold_in(_rk, 12), (64,), 0, 16, jnp.int32)
        return (x, itok_B_0_63, itok_B_0_15)
    x, itok_B_0_63, itok_B_0_15 = _rec_inputs()

    def _L0_cond_setup():
        import jax, jax.numpy as jnp
        import numpy as np
        NUM_CATEGORIES = 64
        INPUT_DIM = 512
        HIDDEN_DIM = 512
        B = 128
        S = 64
        key = jax.random.key(seed)
        kx, kc, kw = jax.random.split(key, 3)
        x = jax.random.normal(kx, (B, S, INPUT_DIM), dtype=jnp.float32)
        cat_ids = jax.random.randint(kc, (B,), 0, NUM_CATEGORIES, dtype=jnp.int32)
        W = 0.02 * jax.random.normal(kw, (NUM_CATEGORIES, INPUT_DIM, HIDDEN_DIM), dtype=jnp.float32)
        b = jnp.zeros((NUM_CATEGORIES, HIDDEN_DIM), dtype=jnp.float32)
        return {'x': x, 'cat_ids': cat_ids, 'W': W, 'b': b}
    _L0_cond_all = _L0_cond_setup()
    _L0_cond_in = {k: v for k, v in _L0_cond_all.items() if k in ('W', 'b')}
    del _L0_cond_all

    def _L1_cond_setup():
        import jax, jax.numpy as jnp
        import numpy as np
        B, N, DIM = (32, 512, 512)
        HID = 2048
        PART = 128
        OUT = 512
        SHARED = OUT - PART
        E = 16
        key = jax.random.key(seed)
        ks = jax.random.split(key, 8)
        s = 0.02
        return {'x': jax.random.normal(ks[0], (B, N, DIM), dtype=jnp.float32), 'indices': jax.random.randint(ks[1], (B,), 0, E, dtype=jnp.int64), 'fc1_w': jax.random.normal(ks[2], (HID, DIM), dtype=jnp.float32) * s, 'fc1_b': jnp.zeros((HID,), dtype=jnp.float32), 'fc2_w': jax.random.normal(ks[3], (SHARED, HID), dtype=jnp.float32) * s, 'fc2_b': jnp.zeros((SHARED,), dtype=jnp.float32), 'experts_w': jax.random.normal(ks[4], (E, PART, HID), dtype=jnp.float32) * s, 'experts_b': jnp.zeros((E, PART), dtype=jnp.float32)}
    _L1_cond_all = _L1_cond_setup()
    _L1_cond_in = {k: v for k, v in _L1_cond_all.items() if k in ('fc1_w', 'fc1_b', 'fc2_w', 'fc2_b', 'experts_w', 'experts_b')}
    del _L1_cond_all
    return {'x': x, 'itok_B_0_63': itok_B_0_63, 'itok_B_0_15': itok_B_0_15, 'L0_cond_W': _L0_cond_in['W'], 'L0_cond_b': _L0_cond_in['b'], 'L1_cond_fc1_w': _L1_cond_in['fc1_w'], 'L1_cond_fc1_b': _L1_cond_in['fc1_b'], 'L1_cond_fc2_w': _L1_cond_in['fc2_w'], 'L1_cond_fc2_b': _L1_cond_in['fc2_b'], 'L1_cond_experts_w': _L1_cond_in['experts_w'], 'L1_cond_experts_b': _L1_cond_in['experts_b']}

def reference(x, itok_B_0_63, itok_B_0_15, L0_cond_W, L0_cond_b, L1_cond_fc1_w, L1_cond_fc1_b, L1_cond_fc2_w, L1_cond_fc2_b, L1_cond_experts_w, L1_cond_experts_b):
    import jax
    import jax.numpy as jnp

    def _L0_cond_ref(x, cat_ids, W, b):
        import jax, jax.numpy as jnp
        import numpy as np
        NUM_CATEGORIES = 64
        INPUT_DIM = 512
        HIDDEN_DIM = 512
        B = 128
        S = 64
        selected_W = W[cat_ids]
        selected_b = b[cat_ids]
        out = jnp.einsum('bsd,bdh->bsh', x, selected_W) + selected_b[:, None, :]
        return out

    def _L1_cond_ref(x, indices, fc1_w, fc1_b, fc2_w, fc2_b, experts_w, experts_b):
        import jax, jax.numpy as jnp
        import numpy as np
        B, N, DIM = (32, 512, 512)
        HID = 2048
        PART = 128
        OUT = 512
        SHARED = OUT - PART
        E = 16
        h = jax.nn.gelu(jnp.einsum('bnd,hd->bnh', x, fc1_w) + fc1_b, approximate=False)
        shared = jnp.einsum('bnh,sh->bns', h, fc2_w) + fc2_b
        We = experts_w[indices]
        be = experts_b[indices]
        expert_x = jnp.einsum('bnh,bph->bnp', h, We) + be[:, None, :]
        return jnp.concatenate([shared, expert_x], axis=-1)
    x = x + _L0_cond_ref(x, itok_B_0_63, L0_cond_W, L0_cond_b)
    x = x + _L1_cond_ref(x, itok_B_0_15, L1_cond_fc1_w, L1_cond_fc1_b, L1_cond_fc2_w, L1_cond_fc2_b, L1_cond_experts_w, L1_cond_experts_b)
    return x

_drawn_inputs = setup_inputs


def setup_inputs(seed=0):
    import zlib

    import numpy as np

    out = dict(_drawn_inputs(seed))
    spreads = {'L0_cond_b': (0.0, 0.1),
     'L1_cond_fc1_b': (0.0, 0.1),
     'L1_cond_fc2_b': (0.0, 0.1),
     'L1_cond_experts_b': (0.0, 0.1)}
    factors = {}
    for name, (base, spread) in spreads.items():
        noise = np.random.default_rng([zlib.crc32(name.encode()), seed]).standard_normal(out[name].shape)
        drawn = base * np.exp(spread * noise) if base else spread * noise
        out[name] = jnp.asarray(drawn.astype(out[name].dtype))
    for name, factor in factors.items():
        out[name] = (out[name] * factor).astype(out[name].dtype)
    return out
```

```python
import concourse.bass as bass
from concourse import mybir
from contextlib import ExitStack

F32 = mybir.dt.float32
F32R = mybir.dt.float32r
I32 = mybir.dt.int32
ALU = mybir.AluOpType
ACT = mybir.ActivationFunctionType
P = 128


def build(nc, x, cat_ids, exp_ids, l0_w, l0_b, fc1_w, fc1_b, fc2_w, fc2_b, exp_w, exp_b, out):
    B, S, D = x.shape
    HID = fc1_w.shape[0]
    SHARED = fc2_w.shape[0]
    PART = exp_w.shape[1]
    assert S == P and PART == P and D == 4 * P and SHARED + PART == D
    GB = 4
    NG = B // GB
    KD = D // P
    NC = HID // P
    assert NC == GB * KD
    NS = SHARED // P
    NQ = HID // D
    PAIR = 2
    NP = NC // PAIR
    WSLOTS = 4
    NPREP = NC + NS * NQ

    ctx = ExitStack()
    with ctx:
        def sb(name, shape, dt=F32):
            return ctx.enter_context(nc.sbuf_tensor(name, shape, dt))

        def pb(name):
            return ctx.enter_context(nc.psum_tensor(name, [P, 512], F32))

        def sem(name):
            return ctx.enter_context(nc.semaphore(name))

        w1 = sb("w1", [P, 2, KD, HID], F32R)
        W2_SIZE = 2 * NC * SHARED
        RING_SIZE = 2 * 2 * (GB // 2) * (3 * P)
        w2e = sb("w2e", [P, W2_SIZE + RING_SIZE], F32R)
        w2 = w2e[:, 0:W2_SIZE].rearrange("p (w c n) -> p w c n", w=2, c=NC)
        ring = w2e[:, W2_SIZE:].rearrange("p (s w q v n) -> p s w q v n", s=2, w=2, q=GB // 2, v=3)
        b1 = sb("b1", [P, NC])
        b1_rows = sb("b1_rows", [NC, P])
        b2_all = sb("b2_all", [P, SHARED])
        ident = sb("ident", [P, P])
        cats = sb("cats", [1, B], I32)
        exps = sb("exps", [1, B], I32)
        w_raw = sb("w_raw", [P, WSLOTS, D])
        w_split = sb("w_split", [P, 2, 2, D], F32R)
        x_raw = sb("x_raw", [P, 2, D])
        x_t = sb("x_t", [P, 2, KD, S], F32R)
        b0_all = sb("b0_all", [P, D])
        y = sb("y", [P, GB, D])
        y_t = sb("y_t", [P, 2, KD, GB, S], F32R)
        g_raw = sb("g_raw", [P, 2, GB * S])
        h = sb("h", [P, 2, 2, GB * S], F32R)
        e_raw = sb("e_raw", [P, 2, GB, PAIR * P])
        be_all = sb("be_all", [P, GB, PART])
        resid = sb("resid", [P, GB, D])

        ps_out = [pb(f"ps_out{b}") for b in range(GB)]
        ps_h = pb("ps_h")
        ps_y = pb("ps_y")
        ps_e = pb("ps_e")
        ps_t = pb("ps_t")

        consts_in = sem("consts_in")
        prep_in = [sem(f"prep_in{i}") for i in range(4)]
        w_in = [sem(f"w_in{i}") for i in range(WSLOTS)]
        x_in = [sem(f"x_in{i}") for i in range(2)]
        b0_in = sem("b0_in")
        be_in = sem("be_in")
        e_in = [sem(f"e_in{i}") for i in range(2)]
        out_stored = sem("out_stored")
        ident_zeroed = sem("ident_zeroed")
        ident_ready = sem("ident_ready")
        xb_ready = sem("xb_ready")
        resid_ready = sem("resid_ready")
        b1_turned = sem("b1_turned")
        prep_turned = sem("prep_turned")
        x_turned = sem("x_turned")
        y_turned = sem("y_turned")
        e_turned = sem("e_turned")
        l0_done = sem("l0_done")
        fc1_done = sem("fc1_done")
        fc2_done = sem("fc2_done")
        b1_ready = sem("b1_ready")
        prep_hi = sem("prep_hi")
        w_hi = sem("w_hi")
        x_hi = sem("x_hi")
        y_hi = sem("y_hi")
        e_hi = sem("e_hi")
        gelu_done = sem("gelu_done")
        prep_lo = sem("prep_lo")
        w_lo = sem("w_lo")
        x_lo = sem("x_lo")
        y_lo = sem("y_lo")
        e_lo = sem("e_lo")
        h_hi = sem("h_hi")
        h_lo = sem("h_lo")
        last_ready = sem("last_ready")
        y_ready = sem("y_ready")
        out_ready = sem("out_ready")

        N_CONST = 5

        def after(eng, s, value):
            if not (isinstance(value, int) and value <= 0):
                eng.wait_ge(s, value)

        def prep_of_step(j):
            lo = NPREP * j // NC
            return range(lo, NPREP * (j + 1) // NC)

        def prep_raw(t):
            return e_raw[:, (t % 4) // 2, 2 * (t % 2):2 * (t % 2) + 2, :].rearrange("p b n -> p (b n)")

        def prep_bank(t):
            return ps_out[t % GB]

        def prep_dst(t, half):
            if t < NC:
                return w1[:, half, :, t * P:(t + 1) * P]
            s, q = (t - NC) // NQ, (t - NC) % NQ
            return w2[:, half, 4 * q:4 * q + 4, s * P:(s + 1) * P]

        def prep_src(t):
            if t < NC:
                return fc1_w[t * P:(t + 1) * P, :]
            s, q = (t - NC) // NQ, (t - NC) % NQ
            return fc2_w[s * P:(s + 1) * P, q * D:(q + 1) * D]

        def experts_of(slot, half):
            return ring[:, slot, half, :, 0:3:2, :]

        def fc2_columns(c, slot, half, b):
            first = (half * NC + c) * SHARED
            second = W2_SIZE + ((slot * 2 + half) * (GB // 2) + b // 2) * 3 * P + (b % 2) * P
            return bass.AP(w2e, first, [[W2_SIZE + RING_SIZE, P], [second - first, 2], [1, 2 * P]])

        def experts_in_bank():
            return ps_e[:, :].rearrange("p (q v n) -> p q v n", q=GB // 2, v=2)

        def four(bank):
            return bank[:, :].rearrange("p (k n) -> p k n", k=4)

        def groups(eng, body):
            body(0, True)
            with eng.Fori(1, NG - 1) as g:
                body(g, True)
            body(NG - 1, False)

        block = ctx.enter_context(nc.Block())

        @block.sync
        def _(sp):
            def index(table, position, count):
                return sp.value_load(table[0:1, bass.ds(position, 1)], min_val=0, max_val=count - 1)

            def load_l0(G, b, k):
                if k == 0:
                    cat = index(cats, G * GB + b, l0_w.shape[0])
                    load_l0.cat = cat
                    after(sp, y_ready, G * GB + b - 1)
                    sp.dma_start(x_raw[:, b % 2, :], x[bass.ds(G * GB + b, 1), :, :].rearrange("o s d -> (o s) d"))\
                      .then_inc(x_in[b % 2], 16)
                    after(sp, xb_ready, G * GB + b)
                    sp.dma_start(b0_all[:, :], l0_b[bass.ds(cat, 1), :].to_broadcast([P, D])).then_inc(b0_in, 16)
                after(sp, w_lo, G * NC + b * KD + k - WSLOTS + 1)
                sp.dma_start(w_raw[:, k, :], l0_w[bass.ds(load_l0.cat, 1), k * P:(k + 1) * P, :]
                             .rearrange("o d n -> (o d) n")).then_inc(w_in[k], 16)

            def load_experts(g, pr, idx):
                after(sp, e_turned, g * NC + PAIR * (pr - 1))
                for b in range(GB):
                    sp.dma_start(e_raw[:, pr % 2, b, :], exp_w[bass.ds(idx[b], 1), :, pr * PAIR * P:(pr + 1) * PAIR * P]
                                 .rearrange("o p n -> (o p) n")).then_inc(e_in[pr % 2], 16)

            def load_expert_bias(G, idx):
                after(sp, resid_ready, G * GB)
                for b in range(GB):
                    sp.dma_start(be_all[:, b, :], exp_b[bass.ds(idx[b], 1), :].to_broadcast([P, PART]))\
                      .then_inc(be_in, 16)

            def store(g):
                for b in range(GB):
                    after(sp, out_ready, g * GB + b + 1)
                    sp.dma_start(out[bass.ds(g * GB + b, 1), :, :].rearrange("o s d -> (o s) d"), resid[:, b, :])\
                      .then_inc(out_stored, 16)

            sp.dma_start(cats[:, :], cat_ids.rearrange("(o n) -> o n", o=1)).then_inc(consts_in, 16)
            sp.dma_start(exps[:, :], exp_ids.rearrange("(o n) -> o n", o=1)).then_inc(consts_in, 16)
            sp.dma_start(b1_rows[:, :], fc1_b.rearrange("(c p) -> c p", p=P)).then_inc(consts_in, 16)
            sp.dma_start(b2_all[:, :], fc2_b.rearrange("(o n) -> o n", o=1).to_broadcast([P, SHARED]))\
              .then_inc(consts_in, 16)
            sp.wait_ge(consts_in, 16 * (N_CONST - 1))
            for j in range(NC):
                load_l0(0, j // KD, j % KD)
                for t in prep_of_step(j):
                    after(sp, prep_turned, t - 3)
                    sp.dma_start(prep_raw(t), prep_src(t)).then_inc(prep_in[t % 4], 16)
            sp.wait_ge(prep_turned, NPREP)

            def body(g, more):
                idx = [index(exps, g * GB + b, exp_w.shape[0]) for b in range(GB)]
                for c in range(NC):
                    if c % PAIR == 1:
                        load_experts(g, c // PAIR, idx)
                    if c == 2:
                        load_expert_bias(g, idx)
                    if c == WSLOTS + 1 and not (isinstance(g, int) and g == 0):
                        store(g - 1)
                    if more:
                        load_l0(g + 1, c // KD, c % KD)
                if not more:
                    store(g)

            groups(sp, body)
            sp.wait_ge(out_stored, 16 * B)

        @block.gpsimd
        def _(pool):
            nc.gpsimd.memset(ident[:, :], 0.0).then_inc(ident_zeroed, 1)
            pool.wait_ge(ident_zeroed, 1)
            nc.gpsimd.affine_select(out=ident[:, :], in_=ident[:, :], compare_op=ALU.not_equal, fill=1.0,
                                    base=0, pattern=[[-1, P]], channel_multiplier=1).then_inc(ident_ready, 1)

            def add_b0(G, b):
                after(pool, x_turned, G * GB + b + 1)
                after(pool, b0_in, 16 * (G * GB + b + 1))
                nc.gpsimd.tensor_tensor(x_raw[:, b % 2, :], x_raw[:, b % 2, :], b0_all[:, :], ALU.add)\
                    .then_inc(xb_ready, 1)

            def add_out_bias(G, b):
                after(pool, y_turned, G * GB + b + 1)
                after(pool, out_stored, G * GB * 16)
                if b == 0:
                    after(pool, be_in, (G + 1) * GB * 16)
                nc.gpsimd.tensor_tensor(resid[:, b, 0:SHARED], y[:, b, 0:SHARED], b2_all[:, :], ALU.add)
                nc.gpsimd.tensor_tensor(resid[:, b, SHARED:D], y[:, b, SHARED:D], be_all[:, b, :], ALU.add)\
                    .then_inc(resid_ready, 1)

            for b in range(GB):
                add_b0(0, b)
            pool.wait_ge(consts_in, 16 * (N_CONST - 1))

            def body(g, more):
                for step, b in (("x", 0), ("y", 0), ("x", 1), ("y", 1), ("y", 2), ("y", 3), ("x", 2), ("x", 3)):
                    if step == "y":
                        add_out_bias(g, b)
                    elif more:
                        add_b0(g + 1, b)

            groups(pool, body)

        @block.scalar
        def _(act):
            def w_high(G, j):
                after(act, w_in[j % WSLOTS], 16 * (G * (NC // WSLOTS) + j // WSLOTS + 1))
                after(act, l0_done, G * NC + j - 1)
                nc.scalar.copy(w_split[:, j % 2, 0, :], w_raw[:, j % WSLOTS, :]).then_inc(w_hi, 1)

            def x_high(G, b):
                after(act, x_turned, G * GB + b + 1)
                after(act, l0_done, G * NC + b * KD)
                nc.scalar.copy(x_t[:, 0, :, :], four(ps_t)).then_inc(x_hi, 1)

            def y_high(G, b):
                after(act, y_turned, G * GB + b + 1)
                nc.scalar.copy(y_t[:, 0, :, b, :], four(ps_t if b % 2 == 0 else ps_e)).then_inc(y_hi, 1)

            def e_high(g, c):
                after(act, e_turned, g * NC + c + 1)
                after(act, fc2_done, (g * NC + c - 1) * GB)
                nc.scalar.copy(experts_of(c % 2, 0), experts_in_bank()).then_inc(e_hi, 1)

            def gelu(g, c):
                after(act, fc1_done, g * NC + c + 1)
                after(act, h_lo, g * NC + c - 1)
                nc.scalar.activation(g_raw[:, c % 2, :], ps_h[:, :], ACT.Gelu, bias=b1[:, c:c + 1])\
                    .then_inc(gelu_done, 1)

            act.wait_ge(b1_turned, 1)
            nc.scalar.copy(b1[:, :], ps_e[:, 0:NC]).then_inc(b1_ready, 1)
            for j in range(NC):
                if j % KD == 0:
                    x_high(0, j // KD)
                w_high(0, j)
                for t in prep_of_step(j):
                    act.wait_ge(prep_turned, t + 1)
                    nc.scalar.copy(prep_dst(t, 0), four(prep_bank(t))).then_inc(prep_hi, 1)
            for b in range(GB):
                y_high(0, b)
            act.wait_ge(b1_ready, 1)

            def body(g, more):
                for c in range(NC):
                    e_high(g, c)
                    if more:
                        if c % KD == 0:
                            x_high(g + 1, c // KD)
                        w_high(g + 1, c)
                    gelu(g, c)
                if more:
                    for b in range(GB):
                        y_high(g + 1, b)

            groups(act, body)

        @block.vector
        def _(dve):
            def minus(dst, whole, high):
                return nc.vector.tensor_tensor(dst, whole, high.bitcast(F32), ALU.subtract)

            def w_low(G, j):
                after(dve, w_hi, G * NC + j + 1)
                minus(w_split[:, j % 2, 1, :], w_raw[:, j % WSLOTS, :], w_split[:, j % 2, 0, :]).then_inc(w_lo, 1)

            def x_low(G, b):
                after(dve, x_hi, G * GB + b + 1)
                minus(x_t[:, 1, :, :], four(ps_t), x_t[:, 0, :, :]).then_inc(x_lo, 1)

            def y_low(G, b):
                after(dve, y_hi, G * GB + b + 1)
                minus(y_t[:, 1, :, b, :], four(ps_t if b % 2 == 0 else ps_e), y_t[:, 0, :, b, :]).then_inc(y_lo, 1)

            def y_sum(G, b):
                after(dve, l0_done, G * NC + (b + 1) * KD)
                after(dve, xb_ready, G * GB + b + 1)
                after(dve, resid_ready, (G - 1) * GB + b + 1)
                nc.vector.tensor_tensor(y[:, b, :], ps_y[:, :], x_raw[:, b % 2, :], ALU.add).then_inc(y_ready, 1)

            def e_low(g, c):
                after(dve, e_hi, g * NC + c + 1)
                minus(experts_of(c % 2, 1), experts_in_bank(), experts_of(c % 2, 0)).then_inc(e_lo, 1)

            def copy_last(g, c):
                after(dve, fc2_done, (g * NC + c - 1) * GB)
                nc.vector.tensor_copy(ring[:, c % 2, :, :, 1, :],
                                      w2[:, :, c, SHARED - P:].unsqueeze(2).to_broadcast([P, 2, GB // 2, P]))\
                    .then_inc(last_ready, 1)

            def h_high(g, c):
                after(dve, gelu_done, g * NC + c + 1)
                after(dve, fc2_done, (g * NC + c - 1) * GB)
                nc.vector.tensor_copy(h[:, c % 2, 0, :], g_raw[:, c % 2, :]).then_inc(h_hi, 1)

            def h_low(g, c):
                after(dve, h_hi, g * NC + c + 1)
                minus(h[:, c % 2, 1, :], g_raw[:, c % 2, :], h[:, c % 2, 0, :]).then_inc(h_lo, 1)

            def result(g, b):
                after(dve, fc2_done, (g * NC + NC - 1) * GB + b + 1)
                after(dve, resid_ready, g * GB + b + 1)
                moves = [(0, 0, D)] if b % 2 else [(0, 0, 2 * P), (2 * P, 3 * P, P), (3 * P, 2 * P, P)]
                for at, bank_at, n in moves:
                    last = nc.vector.tensor_tensor(resid[:, b, at:at + n], ps_out[b][:, bank_at:bank_at + n],
                                                   resid[:, b, at:at + n], ALU.add)
                last.then_inc(out_ready, 1)

            for j in range(NC):
                if j % KD == 0:
                    x_low(0, j // KD)
                w_low(0, j)
                for t in prep_of_step(j):
                    dve.wait_ge(prep_hi, t + 1)
                    minus(prep_dst(t, 1), four(prep_bank(t)), prep_dst(t, 0)).then_inc(prep_lo, 1)
                if j % KD == KD - 1:
                    y_sum(0, j // KD)
            for b in range(GB):
                y_low(0, b)
            dve.wait_ge(prep_lo, NPREP)

            def body(g, more):
                for c in range(NC):
                    copy_last(g, c)
                    e_low(g, c)
                    if more:
                        if c % KD == 0:
                            x_low(g + 1, c // KD)
                        w_low(g + 1, c)
                    h_high(g, c)
                    if more and c % KD == KD - 1:
                        y_sum(g + 1, c // KD)
                    h_low(g, c)
                if more:
                    for b in range(GB):
                        y_low(g + 1, b)
                for b in range(GB):
                    result(g, b)

            groups(dve, body)

        @block.tensor
        def _(pe):
            def turn(bank, tiles):
                for n, tile in enumerate(tiles):
                    last = nc.tensor.transpose(bank[:, n * P:(n + 1) * P], tile, ident[:, :])
                return last

            def turn_x(G, b):
                after(pe, x_in[b % 2], 16 * (G * (GB // 2) + b // 2 + 1))
                if b == 0:
                    after(pe, y_lo, G * GB)
                after(pe, x_lo, G * GB + b)
                turn(ps_t, [x_raw[:, b % 2, k * P:(k + 1) * P] for k in range(KD)]).then_inc(x_turned, 1)

            def turn_y(G, b):
                after(pe, y_ready, G * GB + b + 1)
                if b == 0:
                    after(pe, x_lo, (G + 1) * GB)
                elif b == 1:
                    after(pe, e_lo, G * NC)
                else:
                    after(pe, y_lo, G * GB + b - 1)
                turn(ps_t if b % 2 == 0 else ps_e, [y[:, b, k * P:(k + 1) * P] for k in range(KD)])\
                    .then_inc(y_turned, 1)

            def turn_e(g, c):
                if c % PAIR == 0:
                    pr = c // PAIR
                    after(pe, e_in[pr % 2], 16 * GB * (g * (NP // 2) + pr // 2 + 1))
                if c == 0:
                    after(pe, y_lo, (g + 1) * GB)
                else:
                    after(pe, e_lo, g * NC + c)
                off = (c % PAIR) * P
                turn(ps_e, [e_raw[:, (c // PAIR) % 2, b, off:off + P] for b in range(GB)]).then_inc(e_turned, 1)

            def l0_slice(G, j):
                b, k = j // KD, j % KD
                if k == 0:
                    after(pe, x_lo, G * GB + b + 1)
                    after(pe, y_ready, G * GB + b)
                after(pe, w_lo, G * NC + j + 1)
                for n, (a, w) in enumerate(((0, 0), (0, 1), (1, 0))):
                    last = nc.tensor.matmul(ps_y[:, :], x_t[:, a, k, :], w_split[:, j % 2, w, :],
                                            start=(k == 0 and n == 0), stop=(k == KD - 1 and n == 2))
                last.then_inc(l0_done, 1)

            def fc1(g, c):
                if c == 0:
                    after(pe, y_lo, (g + 1) * GB)
                after(pe, gelu_done, g * NC + c)
                for k in range(KD):
                    for n, (a, w) in enumerate(((0, 0), (1, 0), (0, 1))):
                        last = nc.tensor.matmul(ps_h[:, :], w1[:, w, k, c * P:(c + 1) * P],
                                                y_t[:, a, k, :, :].rearrange("p b s -> p (b s)"),
                                                start=(k == 0 and n == 0), stop=(k == KD - 1 and n == 2))
                last.then_inc(fc1_done, 1)

            def fc2(g, c):
                after(pe, h_lo, g * NC + c + 1)
                after(pe, e_lo, g * NC + c + 1)
                after(pe, last_ready, g * NC + c + 1)
                for b in range(GB):
                    if c == 0:
                        after(pe, out_ready, (g - 1) * GB + b + 1)
                    for n, (a, w) in enumerate(((0, 0), (0, 1), (1, 0))):
                        last = nc.tensor.matmul(ps_out[b][:, :], h[:, c % 2, a, b * S:(b + 1) * S],
                                                fc2_columns(c, c % 2, w, b),
                                                start=(c == 0 and n == 0), stop=(c == NC - 1 and n == 2))
                    last.then_inc(fc2_done, 1)

            pe.wait_ge(ident_ready, 1)
            pe.wait_ge(consts_in, 16 * (N_CONST - 1))
            nc.tensor.transpose(ps_e[:, 0:NC], b1_rows[:, :], ident[0:NC, 0:NC]).then_inc(b1_turned, 1)
            for j in range(NC):
                if j % KD == 0:
                    turn_x(0, j // KD)
                for t in prep_of_step(j):
                    pe.wait_ge(prep_in[t % 4], 16 * (t // 4 + 1))
                    after(pe, prep_lo, t - 3)
                    turn(prep_bank(t), [prep_raw(t)[:, n * P:(n + 1) * P] for n in range(4)]).then_inc(prep_turned, 1)
                l0_slice(0, j)
            pe.wait_ge(b1_ready, 1)
            for b in range(GB):
                turn_y(0, b)
            pe.wait_ge(prep_lo, NPREP)

            def body(g, more):
                for c in range(NC):
                    turn_e(g, c)
                    if more and c % KD == 0:
                        turn_x(g + 1, c // KD)
                    fc1(g, c)
                    if more:
                        l0_slice(g + 1, c)
                    if more and c == NC - 1:
                        turn_y(g + 1, 0)
                        turn_y(g + 1, 1)
                    if c >= 1:
                        fc2(g, c - 1)
                    if more and c == NC - 1:
                        turn_y(g + 1, 2)
                        turn_y(g + 1, 3)
                fc2(g, NC - 1)

            groups(pe, body)


_INS = ["x", "itok_B_0_63", "itok_B_0_15", "L0_cond_W", "L0_cond_b", "L1_cond_fc1_w", "L1_cond_fc1_b",
        "L1_cond_fc2_w", "L1_cond_fc2_b", "L1_cond_experts_w", "L1_cond_experts_b"]


def kernel(**inputs):
    import numpy as np
    import concourse.bacc as bacc
    from concourse.bass_utils import run_bass_kernel_spmd

    nc = bacc.Bacc("TRN2", target_bir_lowering=False, num_devices=1)
    arrays, args = {}, []
    for name in _INS:
        a = np.ascontiguousarray(inputs[name])
        arrays[f"in_{name}"] = a
        args.append(nc.dram_tensor(f"in_{name}", a.shape, mybir.dt.from_np(a.dtype), kind="ExternalInput").ap())
    result = nc.dram_tensor("out_0", arrays["in_x"].shape, F32, kind="ExternalOutput").ap()
    build(nc, *args, result)
    r = run_bass_kernel_spmd(nc, [arrays], core_ids=[0])
    return r.results[0]["out_0"]
```

```python
import concourse.bass as bass
from concourse import mybir
from contextlib import ExitStack

F32 = mybir.dt.float32
F32R = mybir.dt.float32r
I32 = mybir.dt.int32
ALU = mybir.AluOpType
ACT = mybir.ActivationFunctionType
P = 128
DGE_SCRATCH = 1024


def build(nc, x, cat_ids, exp_ids, l0_w, l0_b, fc1_w, fc1_b, fc2_w, fc2_b, exp_w, exp_b, out):
    B, S, D = x.shape
    HID = fc1_w.shape[0]
    SHARED = fc2_w.shape[0]
    PART = exp_w.shape[1]
    assert S == P and PART == P and D == 4 * P and SHARED + PART == D
    GB = 4
    NG = B // GB
    KD = D // P
    NC = HID // P
    assert NC == GB * KD
    NS = SHARED // P
    NQ = HID // D
    PAIR = 2
    NP = NC // PAIR
    WSLOTS = 4
    PSLOTS = 3
    Q = 32
    NPREP = NC + NS * NQ

    NQE = HID // D
    NTURN = exp_w.shape[0] * NQE
    DIRECT = 2
    exp_t = nc.dram_tensor("exp_t", [exp_w.shape[0], P, NC * PART], F32, kind="Internal").ap()

    ctx = ExitStack()
    with ctx:
        def sb(name, shape, dt=F32):
            return ctx.enter_context(nc.sbuf_tensor(name, shape, dt))

        def pb(name):
            return ctx.enter_context(nc.psum_tensor(name, [P, 512], F32))

        def sem(name):
            return ctx.enter_context(nc.semaphore(name))

        w1 = sb("w1", [P, 2, KD, HID], F32R)
        W2_SIZE = 2 * NC * SHARED
        RING_SIZE = 2 * 2 * (GB // 2) * (3 * P)
        w2e = sb("w2e", [P, W2_SIZE + RING_SIZE], F32R)
        w2 = w2e[:, 0:W2_SIZE].rearrange("p (w c n) -> p w c n", w=2, c=NC)
        ring = w2e[:, W2_SIZE:].rearrange("p (s w q v n) -> p s w q v n", s=2, w=2, q=GB // 2, v=3)
        b1 = sb("b1", [P, NC])
        b2_all = sb("b2_all", [P, SHARED])
        ident = sb("ident", [P, P])
        cats = sb("cats", [1, B], I32)
        exps = sb("exps", [1, B], I32)
        w_raw = sb("w_raw", [P, WSLOTS, D])
        w_split = sb("w_split", [P, 2, 2, D], F32R)
        x_raw = sb("x_raw", [P, 2, D])
        x_blocks = sb("x_blocks", [P, D])
        x_whole_t = sb("x_whole_t", [P, D])
        x_t = sb("x_t", [P, 2, KD, S], F32R)
        b0_all = sb("b0_all", [P, D])
        y = sb("y", [P, GB, D])
        y_t = sb("y_t", [P, 2, KD, GB, S], F32R)
        prep_raw = sb("prep_raw", [P, PSLOTS, D])
        g_raw = sb("g_raw", [P, 2, GB * S])
        h = sb("h", [P, 2, 2, GB * S], F32R)
        e_raw = sb("e_raw", [P, 2, GB, PAIR * P])
        turn_in = sb("turn_in", [P, 2, D])
        turn_out = sb("turn_out", [P, 2, D])
        b1_rows = turn_out[0:NC, 0, 0:P]
        resid = sb("resid", [P, GB, D])

        ps_out = [pb(f"ps_out{b}") for b in range(GB)]
        ps_h = pb("ps_h")
        ps_y = pb("ps_y")
        ps_e = pb("ps_e")
        ps_t = pb("ps_t")

        consts_in = sem("consts_in")
        ids_in = sem("ids_in")
        turn_loaded = [sem(f"turn_loaded{i}") for i in range(2)]
        turn_stored = [sem(f"turn_stored{i}") for i in range(2)]
        prep_in = [sem(f"prep_in{i}") for i in range(PSLOTS)]
        w_in = [sem(f"w_in{i}") for i in range(WSLOTS)]
        x_blocks_in = sem("x_blocks_in")
        x_in = [sem(f"x_in{i}") for i in range(2)]
        b0_in = sem("b0_in")
        be_in = sem("be_in")
        e_in = [sem(f"e_in{i}") for i in range(2)]
        out_stored = sem("out_stored")
        ident_zeroed = sem("ident_zeroed")
        ident_ready = sem("ident_ready")
        xb_ready = sem("xb_ready")
        resid_ready = sem("resid_ready")
        b1_turned = sem("b1_turned")
        prep_turned = sem("prep_turned")
        x_turned = sem("x_turned")
        y_turned = sem("y_turned")
        e_turned = sem("e_turned")
        tile_turned = sem("tile_turned")
        l0_done = sem("l0_done")
        fc1_done = sem("fc1_done")
        fc2_done = sem("fc2_done")
        b1_ready = sem("b1_ready")
        prep_hi = sem("prep_hi")
        w_hi = sem("w_hi")
        x_hi = sem("x_hi")
        y_hi = sem("y_hi")
        e_hi = sem("e_hi")
        tile_copied = sem("tile_copied")
        gelu_done = sem("gelu_done")
        prep_lo = sem("prep_lo")
        w_lo = sem("w_lo")
        x_lo = sem("x_lo")
        y_lo = sem("y_lo")
        e_lo = sem("e_lo")
        h_hi = sem("h_hi")
        h_lo = sem("h_lo")
        last_ready = sem("last_ready")
        y_ready = sem("y_ready")
        out_ready = sem("out_ready")


        def after(eng, s, value):
            if not (isinstance(value, int) and value <= 0):
                eng.wait_ge(s, value)

        def fc2_tiles(q):
            return [("fc2", NS - 1, q)] + [("fc2", n, q) for n in range(NS - 1)]

        PREP = ([("fc1", m) for m in range(4)] + fc2_tiles(0) + [("fc1", m) for m in range(4, 8)] + fc2_tiles(1)
                + [("fc1", m) for m in range(8, 11)] + fc2_tiles(2) + [("fc1", m) for m in range(11, 14)]
                + fc2_tiles(3) + [("fc1", m) for m in range(14, NC)])
        PREP_FIRST = NPREP // 2
        assert len(PREP) == NPREP and NPREP - PREP_FIRST <= NC

        def prep_beside(j):
            return range(PSLOTS) if j == 0 else range(j + PSLOTS - 1, min(j + PSLOTS, PREP_FIRST))

        def prep_in_step(g, c):
            return PREP_FIRST + c if isinstance(g, int) and g == 0 and 0 <= c < NPREP - PREP_FIRST else None

        def prep_count(*tile):
            return PREP.index(tile) + 1

        def prep_bank(t):
            return ps_out[t % GB] if t < PREP_FIRST else ps_e

        def prep_dst(t, half):
            if PREP[t][0] == "fc1":
                m = PREP[t][1]
                return w1[:, half, :, m * P:(m + 1) * P]
            _, n, q = PREP[t]
            return w2[:, half, 4 * q:4 * q + 4, n * P:(n + 1) * P]

        def prep_src(t):
            if PREP[t][0] == "fc1":
                m = PREP[t][1]
                return fc1_w[m * P:(m + 1) * P, :]
            _, n, q = PREP[t]
            return fc2_w[n * P:(n + 1) * P, q * D:(q + 1) * D]

        def experts_of(slot, half):
            return ring[:, slot, half, :, 0:3:2, :]

        def fc2_columns(c, slot, half, b):
            first = (half * NC + c) * SHARED
            second = W2_SIZE + ((slot * 2 + half) * (GB // 2) + b // 2) * 3 * P + (b % 2) * P
            return bass.AP(w2e, first, [[W2_SIZE + RING_SIZE, P], [second - first, 2], [1, 2 * P]])

        def experts_arrived(g, pr):
            return 16 * GB * (g * (NP // 2) + pr // 2 + 1)

        def experts_whole(c, direct):
            if direct:
                return ps_e[:, :].rearrange("p (q v n) -> p q v n", q=GB // 2, v=2)
            off = (c % PAIR) * P
            return e_raw[:, (c // PAIR) % 2, :, off:off + P].rearrange("p (q v) n -> p q v n", v=2)

        def h_bank(c, direct):
            return ps_h if direct or c % 2 else ps_e

        def y_bank(G, b):
            return ps_e if b % 2 or (isinstance(G, int) and G == 0) else ps_t

        def turn_steps():
            plan, t = {}, 0
            for g, before, last in ((0, (1, 2, 3, 5, 6, 7, 9, 10), NC), (1, (1, 2, 3), NC - 4)):
                for c in range(last):
                    places = ["before"] * (c in before) + ["after"] + ["within"] * (0 < c < NC - 1)
                    plan[g, c] = {}
                    for place in places:
                        plan[g, c][place] = t
                        t += 1
            assert t == NTURN
            return plan

        TURNS = turn_steps()

        def turn_tile(g, c, place):
            return TURNS.get((g, c), {}).get(place) if isinstance(g, int) else None

        def turned_before(g, c, place=None):
            order = ["before", "after", "within"]
            return sum(1 for (gg, cc), tiles in TURNS.items() for p in tiles
                       if (gg, cc) < (g, c) or ((gg, cc) == (g, c) and place and order.index(p) < order.index(place)))

        def four(bank):
            return bank[:, :].rearrange("p (k n) -> p k n", k=4)

        def groups(eng, body):
            for g in range(DIRECT):
                body(g, True, True)
            with eng.Fori(DIRECT, NG - 1) as g:
                body(g, True, False)
            body(NG - 1, False, False)

        block = ctx.enter_context(nc.Block())

        def load_prep(eng, t):
            if t is None:
                return
            after(eng, prep_turned, t - PSLOTS + 1)
            eng.dma_start(prep_raw[:, t % PSLOTS, :], prep_src(t)).then_inc(prep_in[t % PSLOTS], 16)

        @block.sync
        def _(sp):
            def index(table, position, count):
                return sp.value_load(table[0:1, bass.ds(position, 1)], min_val=0, max_val=count - 1)

            def load_x(G, b):
                after(sp, y_ready, G * GB + b - 1)
                sp.dma_start(x_raw[:, b % 2, :], x[bass.ds(G * GB + b, 1), :, :].rearrange("o s d -> (o s) d"))\
                  .then_inc(x_in[b % 2], 16)

            def load_x_blocks(G, b):
                after(sp, x_turned, G * GB + b)
                for i in range(P // Q):
                    src = x[bass.ds(G * GB + b, 1), :, :].rearrange("o (j q) (k i r) -> i q k (o j) r", q=Q, k=KD, r=Q)[i]
                    sp.dma_start(x_blocks[i * Q:(i + 1) * Q, :].rearrange("q (k j r) -> q k j r", k=KD, r=Q), src)\
                      .then_inc(x_blocks_in, 16)

            def load_l0(G, b, k):
                if k == 0:
                    load_l0.cat = index(cats, G * GB + b, l0_w.shape[0])
                    if not (isinstance(G, int) and G == 0 and b == 0):
                        load_x_blocks(G, b)
                after(sp, w_lo, G * NC + b * KD + k - WSLOTS + 1)
                sp.dma_start(w_raw[:, k, :], l0_w[bass.ds(load_l0.cat, 1), k * P:(k + 1) * P, :]
                             .rearrange("o d n -> (o d) n")).then_inc(w_in[k], 16)
                if k == 0:
                    after(sp, xb_ready, G * GB + b)
                    sp.dma_start(b0_all[:, :], l0_b[bass.ds(load_l0.cat, 1), :].to_broadcast([P, D]))\
                      .then_inc(b0_in, 16)
                if k == 1:
                    load_x(G, b)

            def load_experts(g, pr, idx, direct):
                if direct:
                    after(sp, e_turned, g * NC + PAIR * (pr - 1))
                else:
                    after(sp, e_lo, g * NC + PAIR * (pr - 1))
                source = exp_w if direct else exp_t
                for b in range(GB):
                    sp.dma_start(e_raw[:, pr % 2, b, :], source[bass.ds(idx[b], 1), :, pr * PAIR * P:(pr + 1) * PAIR * P]
                                 .rearrange("o p n -> (o p) n")).then_inc(e_in[pr % 2], 16)

            def load_expert_bias(g, idx):
                after(sp, out_stored, g * GB * 16)
                for b in range(GB):
                    sp.dma_start(resid[:, b, SHARED:D], exp_b[bass.ds(idx[b], 1), :].to_broadcast([P, PART]))\
                      .then_inc(be_in, 16)

            def store(g):
                for b in range(GB):
                    after(sp, out_ready, g * GB + b + 1)
                    sp.dma_start(out[bass.ds(g * GB + b, 1), :, :].rearrange("o s d -> (o s) d"), resid[:, b, :])\
                      .then_inc(out_stored, 16)

            sp.dma_start(cats[:, :], cat_ids.rearrange("(o n) -> o n", o=1)).then_inc(ids_in, 16)
            sp.dma_start(exps[:, :], exp_ids.rearrange("(o n) -> o n", o=1)).then_inc(ids_in, 16)
            load_x_blocks(0, 0)
            sp.wait_ge(ids_in, 16 * 2)
            for j in range(NC):
                load_l0(0, j // KD, j % KD)
                for t in prep_beside(j):
                    if t >= PSLOTS:
                        load_prep(sp, t)
                if j == NC - 6:
                    first_experts = [index(exps, b, exp_w.shape[0]) for b in range(GB)]
                    load_experts(0, 0, first_experts, True)
                if j == 1:
                    sp.dma_start(b1_rows, fc1_b.rearrange("(c p) -> c p", p=P)).then_inc(consts_in, 16)
                    sp.dma_start(b2_all[:, :], fc2_b.rearrange("(o n) -> o n", o=1).to_broadcast([P, SHARED]))\
                      .then_inc(consts_in, 16)
            def body(g, more, direct):
                idx = [index(exps, g * GB + b, exp_w.shape[0]) for b in range(GB)]
                for c in range(NC):
                    if c % PAIR == 1 and not (isinstance(g, int) and (g, c) == (0, 1)):
                        load_experts(g, c // PAIR, idx, direct)
                    load_prep(sp, prep_in_step(g, c - 1))
                    if c == WSLOTS + 1 and not (isinstance(g, int) and g == 0):
                        store(g - 1)
                    if c == WSLOTS + 2:
                        load_expert_bias(g, idx)
                    if more:
                        load_l0(g + 1, c // KD, c % KD)
                if not more:
                    store(g)

            for g in range(DIRECT):
                body(g, True, True)
            for i in range(2):
                sp.wait_ge(turn_stored[i], 16 * (NTURN // 2))
            with sp.Fori(DIRECT, NG - 1) as g:
                body(g, True, False)
            body(NG - 1, False, False)
            sp.wait_ge(out_stored, 16 * B)

        @block.gpsimd
        def _(pool):
            nc.gpsimd.memset(ident[:, :], 0.0).then_inc(ident_zeroed, 1)
            pool.wait_ge(ident_zeroed, 1)
            nc.gpsimd.affine_select(out=ident[:, :], in_=ident[:, :], compare_op=ALU.not_equal, fill=1.0,
                                    base=0, pattern=[[-1, P]], channel_multiplier=1).then_inc(ident_ready, 1)

            def add_b0(G, b):
                after(pool, x_in[b % 2], 16 * (G * (GB // 2) + b // 2 + 1))
                after(pool, b0_in, 16 * (G * GB + b + 1))
                nc.gpsimd.tensor_tensor(x_raw[:, b % 2, :], x_raw[:, b % 2, :], b0_all[:, :], ALU.add)\
                    .then_inc(xb_ready, 1)

            def add_out_bias(G, b):
                after(pool, y_turned, G * GB + b + 1)
                after(pool, out_stored, G * GB * 16)
                if b == 0:
                    after(pool, be_in, (G + 1) * GB * 16)
                nc.gpsimd.tensor_tensor(resid[:, b, 0:SHARED], y[:, b, 0:SHARED], b2_all[:, :], ALU.add)
                nc.gpsimd.tensor_tensor(resid[:, b, SHARED:D], y[:, b, SHARED:D], resid[:, b, SHARED:D], ALU.add)\
                    .then_inc(resid_ready, 1)

            for b in range(GB):
                add_b0(0, b)
            pool.wait_ge(consts_in, 16 * 2)

            def body(g, more, direct):
                for step, b in (("x", 0), ("y", 0), ("x", 1), ("y", 1), ("y", 2), ("y", 3), ("x", 2), ("x", 3)):
                    if step == "y":
                        add_out_bias(g, b)
                    elif more:
                        add_b0(g + 1, b)

            groups(pool, body)

        @block.scalar
        def _(act):
            def w_high(G, j):
                after(act, w_in[j % WSLOTS], 16 * (G * (NC // WSLOTS) + j // WSLOTS + 1))
                after(act, l0_done, G * NC + j - 1)
                nc.scalar.copy(w_split[:, j % 2, 0, :], w_raw[:, j % WSLOTS, :]).then_inc(w_hi, 1)

            def x_high(G, b):
                after(act, x_turned, G * GB + b + 1)
                after(act, l0_done, G * NC + b * KD)
                nc.scalar.copy(x_t[:, 0, :, :], four(x_whole_t)).then_inc(x_hi, 1)

            def y_high(G, b):
                after(act, y_turned, G * GB + b + 1)
                nc.scalar.copy(y_t[:, 0, :, b, :], four(y_bank(G, b))).then_inc(y_hi, 1)

            def e_high(g, c, direct):
                if direct:
                    after(act, e_turned, g * NC + c + 1)
                elif c % PAIR == 0:
                    after(act, e_in[(c // PAIR) % 2], experts_arrived(g, c // PAIR))
                after(act, fc2_done, (g * NC + c - 1) * GB)
                nc.scalar.copy(experts_of(c % 2, 0), experts_whole(c, direct)).then_inc(e_hi, 1)

            def prep_high(t):
                if t is None:
                    return
                act.wait_ge(prep_turned, t + 1)
                nc.scalar.copy(prep_dst(t, 0), four(prep_bank(t))).then_inc(prep_hi, 1)

            def load_tile(t):
                e, q = t // NQE, t % NQE
                act.dma_start(turn_in[:, t % 2, :], exp_w[e, :, q * D:(q + 1) * D]).then_inc(turn_loaded[t % 2], 16)

            def copy_tile(t):
                if t is None:
                    return
                act.wait_ge(tile_turned, t + 1)
                after(act, turn_stored[t % 2], 16 * (t // 2))
                nc.scalar.copy(turn_out[:, t % 2, :], ps_t[:, :]).then_inc(tile_copied, 1)
                if t + 2 < NTURN:
                    load_tile(t + 2)
                act.wait_ge(tile_copied, t + 1)
                e, q = t // NQE, t % NQE
                act.dma_start(exp_t[e, :, q * D:(q + 1) * D], turn_out[:, t % 2, :]).then_inc(turn_stored[t % 2], 16)

            def gelu(g, c, direct):
                after(act, fc1_done, g * NC + c + 1)
                after(act, h_lo, g * NC + c - 1)
                nc.scalar.activation(g_raw[:, c % 2, :], h_bank(c, direct)[:, :], ACT.Gelu, bias=b1[:, c:c + 1])\
                    .then_inc(gelu_done, 1)

            for t in range(PSLOTS):
                load_prep(act, t)
            for j in range(NC):
                if j > 0:
                    w_high(0, j)
                    if j % KD == 0:
                        x_high(0, j // KD)
                for t in prep_beside(j):
                    prep_high(t)
                if j == 0:
                    x_high(0, 0)
                    w_high(0, 0)
                if j == 2:
                    act.wait_ge(b1_turned, 1)
                    nc.scalar.copy(b1[:, :], ps_e[:, 0:NC]).then_inc(b1_ready, 1)
                if j % KD == 0 and j > 0:
                    y_high(0, j // KD - 1)
            load_tile(0)
            load_tile(1)
            y_high(0, GB - 1)
            act.wait_ge(b1_ready, 1)

            def body(g, more, direct):
                for c in range(NC):
                    if more:
                        w_high(g + 1, c)
                        if c % KD == 0:
                            x_high(g + 1, c // KD)
                    e_high(g, c, direct)
                    copy_tile(turn_tile(g, c, "before"))
                    gelu(g, c, direct)
                    prep_high(prep_in_step(g, c))
                    copy_tile(turn_tile(g, c, "after"))
                    copy_tile(turn_tile(g, c, "within"))
                if more:
                    for b in range(GB):
                        y_high(g + 1, b)

            groups(act, body)

        @block.vector
        def _(dve):
            def minus(dst, whole, high):
                return nc.vector.tensor_tensor(dst, whole, high.bitcast(F32), ALU.subtract)

            def prep_low(t):
                if t is None:
                    return
                dve.wait_ge(prep_hi, t + 1)
                minus(prep_dst(t, 1), four(prep_bank(t)), prep_dst(t, 0)).then_inc(prep_lo, 1)

            def w_low(G, j):
                after(dve, w_hi, G * NC + j + 1)
                minus(w_split[:, j % 2, 1, :], w_raw[:, j % WSLOTS, :], w_split[:, j % 2, 0, :]).then_inc(w_lo, 1)

            def turn_x(G, b):
                after(dve, x_blocks_in, 16 * (P // Q) * (G * GB + b + 1))
                after(dve, x_lo, G * GB + b)
                nc.vector.transpose(x_whole_t[:, :], x_blocks[:, :]).then_inc(x_turned, 1)

            def x_low(G, b):
                after(dve, x_hi, G * GB + b + 1)
                minus(x_t[:, 1, :, :], four(x_whole_t), x_t[:, 0, :, :]).then_inc(x_lo, 1)

            def y_low(G, b):
                after(dve, y_hi, G * GB + b + 1)
                minus(y_t[:, 1, :, b, :], four(y_bank(G, b)), y_t[:, 0, :, b, :]).then_inc(y_lo, 1)

            def y_sum(G, b):
                after(dve, l0_done, G * NC + (b + 1) * KD)
                after(dve, xb_ready, G * GB + b + 1)
                after(dve, resid_ready, (G - 1) * GB + b + 1)
                nc.vector.tensor_tensor(y[:, b, :], ps_y[:, :], x_raw[:, b % 2, :], ALU.add).then_inc(y_ready, 1)

            def e_low(g, c, direct):
                after(dve, e_hi, g * NC + c + 1)
                minus(experts_of(c % 2, 1), experts_whole(c, direct), experts_of(c % 2, 0)).then_inc(e_lo, 1)

            def copy_last(g, c):
                after(dve, fc2_done, (g * NC + c - 1) * GB)
                if isinstance(g, int) and g == 0 and c % 4 == 0:
                    dve.wait_ge(prep_lo, prep_count("fc2", NS - 1, c // 4))
                nc.vector.tensor_copy(ring[:, c % 2, :, :, 1, :],
                                      w2[:, :, c, SHARED - P:].unsqueeze(2).to_broadcast([P, 2, GB // 2, P]))\
                    .then_inc(last_ready, 1)

            def h_high(g, c):
                after(dve, gelu_done, g * NC + c + 1)
                after(dve, fc2_done, (g * NC + c - 1) * GB)
                nc.vector.tensor_copy(h[:, c % 2, 0, :], g_raw[:, c % 2, :]).then_inc(h_hi, 1)

            def h_low(g, c):
                after(dve, h_hi, g * NC + c + 1)
                minus(h[:, c % 2, 1, :], g_raw[:, c % 2, :], h[:, c % 2, 0, :]).then_inc(h_lo, 1)

            def result(g, b):
                after(dve, fc2_done, (g * NC + NC - 1) * GB + b + 1)
                after(dve, resid_ready, g * GB + b + 1)
                moves = [(0, 0, D)] if b % 2 else [(0, 0, 2 * P), (2 * P, 3 * P, P), (3 * P, 2 * P, P)]
                for at, bank_at, n in moves:
                    last = nc.vector.tensor_tensor(resid[:, b, at:at + n], ps_out[b][:, bank_at:bank_at + n],
                                                   resid[:, b, at:at + n], ALU.add)
                last.then_inc(out_ready, 1)

            for j in range(NC):
                if j > 0:
                    w_low(0, j)
                    if j % KD == 0:
                        x_low(0, j // KD)
                for t in prep_beside(j):
                    prep_low(t)
                if j == 0:
                    turn_x(0, 0)
                    x_low(0, 0)
                    w_low(0, 0)
                if j % KD == KD - 1:
                    y_sum(0, j // KD)
                    if j + 1 < NC:
                        turn_x(0, j // KD + 1)
                if j % KD == 0 and j > 0:
                    y_low(0, j // KD - 1)
            y_low(0, GB - 1)

            def body(g, more, direct):
                for c in range(NC):
                    if more:
                        if c == 0:
                            turn_x(g + 1, 0)
                        w_low(g + 1, c)
                        if c % KD == 0:
                            x_low(g + 1, c // KD)
                    if c == 1 and not (isinstance(g, int) and g == 0):
                        result(g - 1, 2)
                        result(g - 1, 3)
                    copy_last(g, c)
                    e_low(g, c, direct)
                    if c == 0 and not (isinstance(g, int) and g == 0):
                        result(g - 1, 0)
                        result(g - 1, 1)
                    h_high(g, c)
                    prep_low(prep_in_step(g, c))
                    if more and c % KD == KD - 1:
                        y_sum(g + 1, c // KD)
                    h_low(g, c)
                    if more and c % KD == KD - 1 and c + 1 < NC:
                        turn_x(g + 1, c // KD + 1)
                if more:
                    for b in range(GB):
                        y_low(g + 1, b)

            groups(dve, body)
            for b in range(GB):
                result(NG - 1, b)

        @block.tensor
        def _(pe):
            def turn(bank, tiles):
                for n, tile in enumerate(tiles):
                    last = nc.tensor.transpose(bank[:, n * P:(n + 1) * P], tile, ident[:, :])
                return last

            def turn_y(G, b):
                after(pe, y_ready, G * GB + b + 1)
                if isinstance(G, int) and G == 0:
                    if b == 0:
                        pe.wait_ge(b1_ready, 1)
                    after(pe, y_lo, b)
                elif b == 0:
                    if isinstance(G, int) and G <= DIRECT:
                        pe.wait_ge(tile_copied, turned_before(G, 0))
                elif b == 1:
                    if isinstance(G, int) and G <= DIRECT:
                        after(pe, e_lo, G * NC)
                    else:
                        after(pe, gelu_done, G * NC - 1)
                else:
                    after(pe, y_lo, G * GB + b - 1)
                turn(y_bank(G, b), [y[:, b, k * P:(k + 1) * P] for k in range(KD)])\
                    .then_inc(y_turned, 1)

            def turn_e(g, c):
                if c % PAIR == 0:
                    pr = c // PAIR
                    after(pe, e_in[pr % 2], experts_arrived(g, pr))
                if c == 0:
                    after(pe, y_lo, (g + 1) * GB)
                else:
                    after(pe, e_lo, g * NC + c)
                    if isinstance(g, int) and g == 0:
                        pe.wait_ge(prep_lo, min(PREP_FIRST + c, NPREP))
                off = (c % PAIR) * P
                turn(ps_e, [e_raw[:, (c // PAIR) % 2, b, off:off + P] for b in range(GB)]).then_inc(e_turned, 1)

            def turn_prep(t):
                if t is None:
                    return
                pe.wait_ge(prep_in[t % PSLOTS], 16 * (t // PSLOTS + 1))
                if t < PREP_FIRST:
                    after(pe, prep_lo, t - 3)
                else:
                    pe.wait_ge(e_lo, t - PREP_FIRST + 1)
                turn(prep_bank(t), [prep_raw[:, t % PSLOTS, n * P:(n + 1) * P] for n in range(4)]).then_inc(prep_turned, 1)

            def turn_expert(g, c, place):
                t = turn_tile(g, c, place)
                if t is None:
                    return
                pe.wait_ge(turn_loaded[t % 2], 16 * (t // 2 + 1))
                after(pe, tile_copied, t)
                turn(ps_t, [turn_in[:, t % 2, n * P:(n + 1) * P] for n in range(4)]).then_inc(tile_turned, 1)

            def l0_slice(G, j):
                b, k = j // KD, j % KD
                if k == 0:
                    after(pe, x_lo, G * GB + b + 1)
                    after(pe, y_ready, G * GB + b)
                after(pe, w_lo, G * NC + j + 1)
                for n, (a, w) in enumerate(((0, 0), (0, 1), (1, 0))):
                    last = nc.tensor.matmul(ps_y[:, :], x_t[:, a, k, :], w_split[:, j % 2, w, :],
                                            start=(k == 0 and n == 0), stop=(k == KD - 1 and n == 2))
                last.then_inc(l0_done, 1)

            def fc1(g, c, direct):
                if c == 0:
                    after(pe, y_lo, (g + 1) * GB)
                if isinstance(g, int) and g == 0:
                    pe.wait_ge(prep_lo, prep_count("fc1", c))
                after(pe, gelu_done, g * NC + (c if direct else c - 1))
                for k in range(KD):
                    for n, (a, w) in enumerate(((0, 0), (1, 0), (0, 1))):
                        last = nc.tensor.matmul(h_bank(c, direct)[:, :], w1[:, w, k, c * P:(c + 1) * P],
                                                y_t[:, a, k, :, :].rearrange("p b s -> p (b s)"),
                                                start=(k == 0 and n == 0), stop=(k == KD - 1 and n == 2))
                last.then_inc(fc1_done, 1)

            def fc2(g, c, within=None):
                after(pe, h_lo, g * NC + c + 1)
                after(pe, e_lo, g * NC + c + 1)
                after(pe, last_ready, g * NC + c + 1)
                if isinstance(g, int) and g == 0 and c % 4 == 0:
                    pe.wait_ge(prep_lo, prep_count("fc2", NS - 2, c // 4))
                for b in range(GB):
                    if c == 0:
                        after(pe, out_ready, (g - 1) * GB + b + 1)
                    for n, (a, w) in enumerate(((0, 0), (0, 1), (1, 0))):
                        last = nc.tensor.matmul(ps_out[b][:, :], h[:, c % 2, a, b * S:(b + 1) * S],
                                                fc2_columns(c, c % 2, w, b),
                                                start=(c == 0 and n == 0), stop=(c == NC - 1 and n == 2))
                    last.then_inc(fc2_done, 1)
                    if b == 1 and within is not None:
                        turn_expert(*within, "within")

            pe.wait_ge(ident_ready, 1)
            for j in range(NC):
                for t in prep_beside(j):
                    turn_prep(t)
                if j % KD == 0 and j > 0:
                    turn_y(0, j // KD - 1)
                l0_slice(0, j)
                if j == 2:
                    pe.wait_ge(consts_in, 16 * 2)
                    nc.tensor.transpose(ps_e[:, 0:NC], b1_rows, ident[0:NC, 0:NC]).then_inc(b1_turned, 1)
            turn_y(0, GB - 1)

            def body(g, more, direct):
                for c in range(NC):
                    if direct:
                        turn_e(g, c)
                        turn_expert(g, c, "before")
                    fc1(g, c, direct)
                    turn_prep(prep_in_step(g, c))
                    turn_expert(g, c, "after")
                    if more:
                        l0_slice(g + 1, c)
                    if more and c == NC - 1:
                        turn_y(g + 1, 0)
                        turn_y(g + 1, 1)
                    if c >= 1:
                        fc2(g, c - 1, within=(g, c))
                    if more and c == NC - 1:
                        turn_y(g + 1, 2)
                        turn_y(g + 1, 3)
                fc2(g, NC - 1)

            groups(pe, body)


_INS = ["x", "itok_B_0_63", "itok_B_0_15", "L0_cond_W", "L0_cond_b", "L1_cond_fc1_w", "L1_cond_fc1_b",
        "L1_cond_fc2_w", "L1_cond_fc2_b", "L1_cond_experts_w", "L1_cond_experts_b"]


def kernel(**inputs):
    import numpy as np
    import concourse.bacc as bacc
    from concourse.bass_utils import run_bass_kernel_spmd

    nc = bacc.Bacc("TRN2", target_bir_lowering=False, num_devices=1, dynamic_dma_scratch_size=DGE_SCRATCH)
    arrays, args = {}, []
    for name in _INS:
        a = np.ascontiguousarray(inputs[name])
        arrays[f"in_{name}"] = a
        args.append(nc.dram_tensor(f"in_{name}", a.shape, mybir.dt.from_np(a.dtype), kind="ExternalInput").ap())
    result = nc.dram_tensor("out_0", arrays["in_x"].shape, F32, kind="ExternalOutput").ap()
    build(nc, *args, result)
    r = run_bass_kernel_spmd(nc, [arrays], core_ids=[0])
    return r.results[0]["out_0"]
```

```python
import concourse.bass as bass
from concourse import mybir
from contextlib import ExitStack

F32 = mybir.dt.float32
F32R = mybir.dt.float32r
I32 = mybir.dt.int32
ALU = mybir.AluOpType
ACT = mybir.ActivationFunctionType
P = 128
DGE_SCRATCH = 1024


def build(nc, x, cat_ids, exp_ids, l0_w, l0_b, fc1_w, fc1_b, fc2_w, fc2_b, exp_w, exp_b, out):
    B, S, D = x.shape
    HID = fc1_w.shape[0]
    SHARED = fc2_w.shape[0]
    PART = exp_w.shape[1]
    assert S == P and PART == P and D == 4 * P and SHARED + PART == D
    GB = 4
    NG = B // GB
    KD = D // P
    NC = HID // P
    assert NC == GB * KD
    NS = SHARED // P
    NQ = HID // D
    PAIR = 2
    NP = NC // PAIR
    WSLOTS = 4
    PSLOTS = 3
    Q = 32
    NPREP = NC + NS * NQ

    NQE = HID // D
    NTURN = exp_w.shape[0] * NQE
    DIRECT = 2
    exp_t = nc.dram_tensor("exp_t", [exp_w.shape[0], P, NC * PART], F32, kind="Internal").ap()

    ctx = ExitStack()
    with ctx:
        def sb(name, shape, dt=F32):
            return ctx.enter_context(nc.sbuf_tensor(name, shape, dt))

        def pb(name):
            return ctx.enter_context(nc.psum_tensor(name, [P, 512], F32))

        def sem(name):
            return ctx.enter_context(nc.semaphore(name))

        w1 = sb("w1", [P, 2, KD, HID], F32R)
        W2_SIZE = 2 * NC * SHARED
        RING_SIZE = 2 * 2 * (GB // 2) * (3 * P)
        w2e = sb("w2e", [P, W2_SIZE + RING_SIZE], F32R)
        w2 = w2e[:, 0:W2_SIZE].rearrange("p (w c n) -> p w c n", w=2, c=NC)
        ring = w2e[:, W2_SIZE:].rearrange("p (s w q v n) -> p s w q v n", s=2, w=2, q=GB // 2, v=3)
        b1 = sb("b1", [P, NC])
        b2_all = sb("b2_all", [P, SHARED])
        ident = sb("ident", [P, P])
        cats = sb("cats", [1, B], I32)
        exps = sb("exps", [1, B], I32)
        w_raw = sb("w_raw", [P, WSLOTS, D])
        w_split = sb("w_split", [P, 2, 2, D], F32R)
        x_raw = sb("x_raw", [P, 2, D])
        x_blocks = sb("x_blocks", [P, D])
        x_whole_t = sb("x_whole_t", [P, D])
        x_t = sb("x_t", [P, 2, KD, S], F32R)
        b0_all = sb("b0_all", [P, D])
        y = sb("y", [P, GB, D])
        y_t = sb("y_t", [P, 2, KD, GB, S], F32R)
        prep_raw = sb("prep_raw", [P, PSLOTS, D])
        g_raw = sb("g_raw", [P, 2, GB * S])
        h = sb("h", [P, 2, 2, GB * S], F32R)
        e_raw = sb("e_raw", [P, 2, GB, PAIR * P])
        turn_in = sb("turn_in", [P, 2, D])
        turn_out = sb("turn_out", [P, 2, D])
        b1_rows = turn_out[0:NC, 0, 0:P]
        resid = sb("resid", [P, GB, D])

        ps_out = [pb(f"ps_out{b}") for b in range(GB)]
        ps_h = pb("ps_h")
        ps_y = pb("ps_y")
        ps_e = pb("ps_e")
        ps_t = pb("ps_t")

        consts_in = sem("consts_in")
        cats_in = sem("cats_in")
        exps_in = sem("exps_in")
        turn_loaded = [sem(f"turn_loaded{i}") for i in range(2)]
        turn_stored = [sem(f"turn_stored{i}") for i in range(2)]
        prep_in = [sem(f"prep_in{i}") for i in range(PSLOTS)]
        w_in = [sem(f"w_in{i}") for i in range(WSLOTS)]
        x_blocks_in = sem("x_blocks_in")
        x_in = [sem(f"x_in{i}") for i in range(2)]
        first_x_in = [sem(f"first_x_in{b}") for b in range(GB)]
        b0_in = sem("b0_in")
        be_in = sem("be_in")
        e_in = [sem(f"e_in{i}") for i in range(2)]
        out_stored = sem("out_stored")
        ident_zeroed = sem("ident_zeroed")
        ident_ready = sem("ident_ready")
        xb_ready = sem("xb_ready")
        resid_ready = sem("resid_ready")
        b1_turned = sem("b1_turned")
        prep_turned = sem("prep_turned")
        x_turned = sem("x_turned")
        y_turned = sem("y_turned")
        e_turned = sem("e_turned")
        tile_turned = sem("tile_turned")
        l0_done = sem("l0_done")
        fc1_done = sem("fc1_done")
        fc2_done = sem("fc2_done")
        b1_ready = sem("b1_ready")
        prep_hi = sem("prep_hi")
        w_hi = sem("w_hi")
        x_hi = sem("x_hi")
        y_hi = sem("y_hi")
        e_hi = sem("e_hi")
        tile_copied = sem("tile_copied")
        gelu_done = sem("gelu_done")
        prep_lo = sem("prep_lo")
        w_lo = sem("w_lo")
        x_lo = sem("x_lo")
        y_lo = sem("y_lo")
        e_lo = sem("e_lo")
        h_hi = sem("h_hi")
        h_lo = sem("h_lo")
        last_ready = sem("last_ready")
        y_ready = sem("y_ready")
        out_ready = sem("out_ready")

        def after(eng, s, value):
            if not (isinstance(value, int) and value <= 0):
                eng.wait_ge(s, value)

        def first(G):
            return isinstance(G, int) and G == 0

        def fc2_tiles(q):
            return [("fc2", NS - 1, q)] + [("fc2", n, q) for n in range(NS - 1)]

        PREP = ([("fc1", m) for m in range(4)] + fc2_tiles(0) + [("fc1", m) for m in range(4, 8)] + fc2_tiles(1)
                + [("fc1", m) for m in range(8, 11)] + fc2_tiles(2) + [("fc1", m) for m in range(11, 14)]
                + fc2_tiles(3) + [("fc1", m) for m in range(14, NC)])
        PREP_FIRST = NPREP // 2 - 1
        assert len(PREP) == NPREP and NPREP - PREP_FIRST <= NC

        def prep_beside(j):
            return range(PSLOTS) if j == 0 else range(j + PSLOTS - 1, min(j + PSLOTS, PREP_FIRST))

        def prep_in_step(g, c):
            return PREP_FIRST + c if first(g) and 0 <= c < NPREP - PREP_FIRST else None

        def prep_count(*tile):
            return PREP.index(tile) + 1

        def prep_bank(t):
            return ps_out[t % GB] if t < PREP_FIRST else ps_e

        def prep_dst(t, half):
            if PREP[t][0] == "fc1":
                m = PREP[t][1]
                return w1[:, half, :, m * P:(m + 1) * P]
            _, n, q = PREP[t]
            return w2[:, half, 4 * q:4 * q + 4, n * P:(n + 1) * P]

        def prep_src(t):
            if PREP[t][0] == "fc1":
                m = PREP[t][1]
                return fc1_w[m * P:(m + 1) * P, :]
            _, n, q = PREP[t]
            return fc2_w[n * P:(n + 1) * P, q * D:(q + 1) * D]

        def experts_of(slot, half):
            return ring[:, slot, half, :, 0:3:2, :]

        def fc2_columns(c, slot, half, b):
            shared = (half * NC + c) * SHARED
            second = W2_SIZE + ((slot * 2 + half) * (GB // 2) + b // 2) * 3 * P + (b % 2) * P
            return bass.AP(w2e, shared, [[W2_SIZE + RING_SIZE, P], [second - shared, 2], [1, 2 * P]])

        def experts_arrived(g, pr):
            return 16 * GB * (g * (NP // 2) + pr // 2 + 1)

        def experts_whole(c, direct):
            if direct:
                return ps_e[:, :].rearrange("p (q v n) -> p q v n", q=GB // 2, v=2)
            off = (c % PAIR) * P
            return e_raw[:, (c // PAIR) % 2, :, off:off + P].rearrange("p (q v) n -> p q v n", v=2)

        def h_bank(c, direct):
            return ps_h if direct or c % 2 else ps_e

        def x_whole(G):
            return four(ps_t if first(G) else x_whole_t)

        def x_halves(G, b):
            return h[:, 1, :, :].rearrange("p w (k s) -> p w k s", k=KD) if first(G) and b % 2 else x_t

        def l0_bank(G, b):
            return ps_h if first(G) and b % 2 else ps_y

        def y_bank(G, b):
            if first(G):
                return ps_y if b == GB - 1 else ps_e
            return ps_e if b % 2 else ps_t

        def turn_steps():
            plan, t = {}, 0
            for g, before, last in ((0, (2, 6, 7, 9, 10), NC), (1, (1, 2, 3, 5, 6, 7), NC - 4)):
                for c in range(last):
                    places = ["before"] * (c in before) + ["after"] + ["within"] * (0 < c < NC - 1)
                    plan[g, c] = {}
                    for place in places:
                        plan[g, c][place] = t
                        t += 1
            assert t == NTURN
            return plan

        TURNS = turn_steps()

        def turn_tile(g, c, place):
            return TURNS.get((g, c), {}).get(place) if isinstance(g, int) else None

        def turned_before(g, c):
            return sum(len(tiles) for step, tiles in TURNS.items() if step < (g, c))

        def four(bank):
            return bank[:, :].rearrange("p (k n) -> p k n", k=4)

        def groups(eng, body):
            for g in range(DIRECT):
                body(g, True, True)
            with eng.Fori(DIRECT, NG - 1) as g:
                body(g, True, False)
            body(NG - 1, False, False)

        block = ctx.enter_context(nc.Block())

        def load_prep(eng, t):
            if t is None:
                return
            after(eng, prep_turned, t - PSLOTS + 1)
            eng.dma_start(prep_raw[:, t % PSLOTS, :], prep_src(t)).then_inc(prep_in[t % PSLOTS], 16)

        @block.sync
        def _(sp):
            def index(table, position, count):
                return sp.value_load(table[0:1, bass.ds(position, 1)], min_val=0, max_val=count - 1)

            def load_x(G, b):
                after(sp, y_ready, G * GB + b - 1)
                sp.dma_start(x_raw[:, b % 2, :], x[bass.ds(G * GB + b, 1), :, :].rearrange("o s d -> (o s) d"))\
                  .then_inc(x_in[b % 2], 16)

            def load_first_x(b):
                sp.dma_start(resid[:, b, :], x[b, :, :]).then_inc(first_x_in[b], 16)

            def load_x_blocks(G, b):
                after(sp, x_turned, G * GB + b)
                for i in range(P // Q):
                    src = x[bass.ds(G * GB + b, 1), :, :].rearrange("o (j q) (k i r) -> i q k (o j) r", q=Q, k=KD, r=Q)[i]
                    sp.dma_start(x_blocks[i * Q:(i + 1) * Q, :].rearrange("q (k j r) -> q k j r", k=KD, r=Q), src)\
                      .then_inc(x_blocks_in, 16)

            def load_l0(G, b, k):
                if k == 0:
                    load_l0.cat = index(cats, G * GB + b, l0_w.shape[0])
                    if not first(G):
                        load_x_blocks(G, b)
                after(sp, w_lo, G * NC + b * KD + k - WSLOTS + 1)
                sp.dma_start(w_raw[:, k, :], l0_w[bass.ds(load_l0.cat, 1), k * P:(k + 1) * P, :]
                             .rearrange("o d n -> (o d) n")).then_inc(w_in[k], 16)
                if k == 0:
                    after(sp, xb_ready, G * GB + b)
                    sp.dma_start(b0_all[:, :], l0_b[bass.ds(load_l0.cat, 1), :].to_broadcast([P, D]))\
                      .then_inc(b0_in, 16)
                if k == 1 and not first(G):
                    load_x(G, b)

            def load_experts(g, pr, idx, direct):
                if direct:
                    after(sp, e_turned, g * NC + PAIR * (pr - 1))
                else:
                    after(sp, e_lo, g * NC + PAIR * (pr - 1))
                source = exp_w if direct else exp_t
                for b in range(GB):
                    sp.dma_start(e_raw[:, pr % 2, b, :], source[bass.ds(idx[b], 1), :, pr * PAIR * P:(pr + 1) * PAIR * P]
                                 .rearrange("o p n -> (o p) n")).then_inc(e_in[pr % 2], 16)

            def load_expert_bias(g, idx):
                if first(g):
                    sp.wait_ge(x_turned, GB)
                    sp.wait_ge(xb_ready, GB)
                after(sp, out_stored, g * GB * 16)
                for b in range(GB):
                    sp.dma_start(resid[:, b, SHARED:D], exp_b[bass.ds(idx[b], 1), :].to_broadcast([P, PART]))\
                      .then_inc(be_in, 16)

            def store(g):
                for b in range(GB):
                    after(sp, out_ready, g * GB + b + 1)
                    sp.dma_start(out[bass.ds(g * GB + b, 1), :, :].rearrange("o s d -> (o s) d"), resid[:, b, :])\
                      .then_inc(out_stored, 16)

            sp.dma_start(cats[:, :], cat_ids.rearrange("(o n) -> o n", o=1)).then_inc(cats_in, 16)
            load_first_x(0)
            sp.wait_ge(cats_in, 16)
            first_experts = []
            for j in range(NC):
                load_l0(0, j // KD, j % KD)
                for t in prep_beside(j):
                    if t >= PSLOTS:
                        load_prep(sp, t)
                if j % KD == KD - 2 and j // KD + 1 < GB:
                    load_first_x(j // KD + 1)
                if j == KD:
                    sp.wait_ge(exps_in, 16)
                if KD <= j < KD + GB:
                    first_experts.append(index(exps, j - KD, exp_w.shape[0]))
                if j == NC - 2:
                    load_experts(0, 0, first_experts, True)
                if j == 1:
                    sp.dma_start(exps[:, :], exp_ids.rearrange("(o n) -> o n", o=1)).then_inc(exps_in, 16)
                    sp.dma_start(b1_rows, fc1_b.rearrange("(c p) -> c p", p=P)).then_inc(consts_in, 16)
                    sp.dma_start(b2_all[:, :], fc2_b.rearrange("(o n) -> o n", o=1).to_broadcast([P, SHARED]))\
                      .then_inc(consts_in, 16)

            def body(g, more, direct):
                idx = first_experts if first(g) else [index(exps, g * GB + b, exp_w.shape[0]) for b in range(GB)]
                for c in range(NC):
                    if c % PAIR == 1 and not (first(g) and c == 1):
                        load_experts(g, c // PAIR, idx, direct)
                    load_prep(sp, prep_in_step(g, c))
                    if c == WSLOTS and not first(g):
                        store(g - 1)
                    if c == (2 if first(g) else WSLOTS + 1):
                        load_expert_bias(g, idx)
                    if more:
                        load_l0(g + 1, c // KD, c % KD)
                if not more:
                    store(g)

            for g in range(DIRECT):
                body(g, True, True)
            for i in range(2):
                sp.wait_ge(turn_stored[i], 16 * (NTURN // 2))
            with sp.Fori(DIRECT, NG - 1) as g:
                body(g, True, False)
            body(NG - 1, False, False)
            sp.wait_ge(out_stored, 16 * B)

        @block.gpsimd
        def _(pool):
            nc.gpsimd.memset(ident[:, :], 0.0).then_inc(ident_zeroed, 1)
            pool.wait_ge(ident_zeroed, 1)
            nc.gpsimd.affine_select(out=ident[:, :], in_=ident[:, :], compare_op=ALU.not_equal, fill=1.0,
                                    base=0, pattern=[[-1, P]], channel_multiplier=1).then_inc(ident_ready, 1)

            def add_b0(G, b):
                if first(G):
                    pool.wait_ge(first_x_in[b], 16)
                    after(pool, y_ready, b - 1)
                    source = resid[:, b, :]
                else:
                    after(pool, x_in[b % 2], 16 * ((G - 1) * (GB // 2) + b // 2 + 1))
                    source = x_raw[:, b % 2, :]
                after(pool, b0_in, 16 * (G * GB + b + 1))
                nc.gpsimd.tensor_tensor(x_raw[:, b % 2, :], source, b0_all[:, :], ALU.add).then_inc(xb_ready, 1)

            def add_out_bias(G, b):
                after(pool, y_turned, G * GB + b + 1)
                after(pool, out_stored, G * GB * 16)
                if b == 0:
                    after(pool, be_in, (G + 1) * GB * 16)
                nc.gpsimd.tensor_tensor(resid[:, b, 0:SHARED], y[:, b, 0:SHARED], b2_all[:, :], ALU.add)
                nc.gpsimd.tensor_tensor(resid[:, b, SHARED:D], y[:, b, SHARED:D], resid[:, b, SHARED:D], ALU.add)\
                    .then_inc(resid_ready, 1)

            for b in range(GB):
                add_b0(0, b)
            pool.wait_ge(consts_in, 16 * 2)

            def body(g, more, direct):
                for step, b in (("x", 0), ("y", 0), ("x", 1), ("y", 1), ("y", 2), ("y", 3), ("x", 2), ("x", 3)):
                    if step == "y":
                        add_out_bias(g, b)
                    elif more:
                        add_b0(g + 1, b)

            groups(pool, body)

        @block.scalar
        def _(act):
            def w_high(G, j):
                after(act, w_in[j % WSLOTS], 16 * (G * (NC // WSLOTS) + j // WSLOTS + 1))
                after(act, l0_done, G * NC + j - 1)
                nc.scalar.copy(w_split[:, j % 2, 0, :], w_raw[:, j % WSLOTS, :]).then_inc(w_hi, 1)

            def x_high(G, b):
                after(act, x_turned, G * GB + b + 1)
                after(act, l0_done, G * NC + (b - 1 if first(G) else b) * KD)
                nc.scalar.copy(x_halves(G, b)[:, 0, :, :], x_whole(G)).then_inc(x_hi, 1)

            def y_high(G, b):
                after(act, y_turned, G * GB + b + 1)
                nc.scalar.copy(y_t[:, 0, :, b, :], four(y_bank(G, b))).then_inc(y_hi, 1)

            def e_high(g, c, direct):
                if direct:
                    after(act, e_turned, g * NC + c + 1)
                elif c % PAIR == 0:
                    after(act, e_in[(c // PAIR) % 2], experts_arrived(g, c // PAIR))
                after(act, fc2_done, (g * NC + c - 1) * GB)
                nc.scalar.copy(experts_of(c % 2, 0), experts_whole(c, direct)).then_inc(e_hi, 1)

            def prep_high(t):
                if t is None:
                    return
                act.wait_ge(prep_turned, t + 1)
                nc.scalar.copy(prep_dst(t, 0), four(prep_bank(t))).then_inc(prep_hi, 1)

            def load_tile(t):
                e, q = t // NQE, t % NQE
                act.dma_start(turn_in[:, t % 2, :], exp_w[e, :, q * D:(q + 1) * D]).then_inc(turn_loaded[t % 2], 16)

            def copy_tile(t):
                if t is None:
                    return
                act.wait_ge(tile_turned, t + 1)
                after(act, turn_stored[t % 2], 16 * (t // 2))
                nc.scalar.copy(turn_out[:, t % 2, :], ps_t[:, :]).then_inc(tile_copied, 1)
                if t + 2 < NTURN:
                    load_tile(t + 2)
                act.wait_ge(tile_copied, t + 1)
                e, q = t // NQE, t % NQE
                act.dma_start(exp_t[e, :, q * D:(q + 1) * D], turn_out[:, t % 2, :]).then_inc(turn_stored[t % 2], 16)

            def gelu(g, c, direct):
                after(act, fc1_done, g * NC + c + 1)
                after(act, h_lo, g * NC + c - 1)
                nc.scalar.activation(g_raw[:, c % 2, :], h_bank(c, direct)[:, :], ACT.Gelu, bias=b1[:, c:c + 1])\
                    .then_inc(gelu_done, 1)

            for t in range(PSLOTS):
                load_prep(act, t)
            act.wait_ge(ident_ready, 1)
            nc.scalar.activation(g_raw[:, 0, 0:1], ident[:, 0:1], ACT.Gelu)
            for j in range(NC):
                if j > 0 and j + 1 < NC:
                    w_high(0, j + 1)
                if j % KD == 1 and j > KD:
                    y_high(0, j // KD - 1)
                if j % KD == KD - 1 and j + 1 < NC:
                    x_high(0, j // KD + 1)
                for t in prep_beside(j):
                    if t == PSLOTS - 1:
                        x_high(0, 0)
                        w_high(0, 0)
                        w_high(0, 1)
                    prep_high(t)
                if j == 2:
                    act.wait_ge(b1_turned, 1)
                    nc.scalar.copy(b1[:, :], ps_e[:, 0:NC]).then_inc(b1_ready, 1)
            load_tile(0)
            load_tile(1)
            y_high(0, GB - 1)
            act.wait_ge(b1_ready, 1)

            def body(g, more, direct):
                for c in range(NC):
                    if more:
                        w_high(g + 1, c)
                        if c % KD == 0:
                            x_high(g + 1, c // KD)
                    e_high(g, c, direct)
                    copy_tile(turn_tile(g, c, "before"))
                    gelu(g, c, direct)
                    prep_high(prep_in_step(g, c))
                    copy_tile(turn_tile(g, c, "after"))
                    copy_tile(turn_tile(g, c, "within"))
                if more:
                    for b in range(GB):
                        y_high(g + 1, b)

            groups(act, body)

        @block.vector
        def _(dve):
            def minus(dst, whole, high):
                return nc.vector.tensor_tensor(dst, whole, high.bitcast(F32), ALU.subtract)

            def prep_low(t):
                if t is None:
                    return
                dve.wait_ge(prep_hi, t + 1)
                minus(prep_dst(t, 1), four(prep_bank(t)), prep_dst(t, 0)).then_inc(prep_lo, 1)

            def w_low(G, j):
                after(dve, w_hi, G * NC + j + 1)
                minus(w_split[:, j % 2, 1, :], w_raw[:, j % WSLOTS, :], w_split[:, j % 2, 0, :]).then_inc(w_lo, 1)

            def turn_x(G, b):
                after(dve, x_blocks_in, 16 * (P // Q) * ((G - 1) * GB + b + 1))
                after(dve, x_lo, G * GB + b)
                nc.vector.transpose(x_whole_t[:, :], x_blocks[:, :]).then_inc(x_turned, 1)

            def x_low(G, b):
                after(dve, x_hi, G * GB + b + 1)
                minus(x_halves(G, b)[:, 1, :, :], x_whole(G), x_halves(G, b)[:, 0, :, :]).then_inc(x_lo, 1)

            def y_low(G, b):
                after(dve, y_hi, G * GB + b + 1)
                minus(y_t[:, 1, :, b, :], four(y_bank(G, b)), y_t[:, 0, :, b, :]).then_inc(y_lo, 1)

            def y_sum(G, b):
                after(dve, l0_done, G * NC + (b + 1) * KD)
                after(dve, xb_ready, G * GB + b + 1)
                after(dve, resid_ready, (G - 1) * GB + b + 1)
                nc.vector.tensor_tensor(y[:, b, :], l0_bank(G, b)[:, :], x_raw[:, b % 2, :], ALU.add).then_inc(y_ready, 1)

            def e_low(g, c, direct):
                after(dve, e_hi, g * NC + c + 1)
                minus(experts_of(c % 2, 1), experts_whole(c, direct), experts_of(c % 2, 0)).then_inc(e_lo, 1)

            def copy_last(g, c):
                after(dve, fc2_done, (g * NC + c - 1) * GB)
                if first(g) and c % 4 == 0:
                    dve.wait_ge(prep_lo, prep_count("fc2", NS - 1, c // 4))
                nc.vector.tensor_copy(ring[:, c % 2, :, :, 1, :],
                                      w2[:, :, c, SHARED - P:].unsqueeze(2).to_broadcast([P, 2, GB // 2, P]))\
                    .then_inc(last_ready, 1)

            def h_high(g, c):
                after(dve, gelu_done, g * NC + c + 1)
                after(dve, fc2_done, (g * NC + c - 1) * GB)
                nc.vector.tensor_copy(h[:, c % 2, 0, :], g_raw[:, c % 2, :]).then_inc(h_hi, 1)

            def h_low(g, c):
                after(dve, h_hi, g * NC + c + 1)
                minus(h[:, c % 2, 1, :], g_raw[:, c % 2, :], h[:, c % 2, 0, :]).then_inc(h_lo, 1)

            def result(g, b):
                after(dve, fc2_done, (g * NC + NC - 1) * GB + b + 1)
                after(dve, resid_ready, g * GB + b + 1)
                moves = [(0, 0, D)] if b % 2 else [(0, 0, 2 * P), (2 * P, 3 * P, P), (3 * P, 2 * P, P)]
                for at, bank_at, n in moves:
                    last = nc.vector.tensor_tensor(resid[:, b, at:at + n], ps_out[b][:, bank_at:bank_at + n],
                                                   resid[:, b, at:at + n], ALU.add)
                last.then_inc(out_ready, 1)

            for j in range(NC):
                if j > 0 and j + 1 < NC:
                    w_low(0, j + 1)
                if j % KD == 1 and j > KD:
                    y_low(0, j // KD - 1)
                if j % KD == KD - 1 and j + 1 < NC:
                    x_low(0, j // KD + 1)
                for t in prep_beside(j):
                    if t == PSLOTS - 1:
                        x_low(0, 0)
                        w_low(0, 0)
                        w_low(0, 1)
                    prep_low(t)
                if j % KD == KD - 1:
                    y_sum(0, j // KD)
            y_low(0, GB - 1)

            def body(g, more, direct):
                for c in range(NC):
                    if more:
                        if c == 0:
                            turn_x(g + 1, 0)
                        w_low(g + 1, c)
                        if c % KD == 0:
                            x_low(g + 1, c // KD)
                    if c == 1 and not first(g):
                        result(g - 1, 2)
                        result(g - 1, 3)
                    copy_last(g, c)
                    e_low(g, c, direct)
                    if c == 0 and not first(g):
                        result(g - 1, 0)
                        result(g - 1, 1)
                    h_high(g, c)
                    prep_low(prep_in_step(g, c))
                    if more and c % KD == KD - 1:
                        y_sum(g + 1, c // KD)
                    h_low(g, c)
                    if more and c % KD == KD - 1 and c + 1 < NC:
                        turn_x(g + 1, c // KD + 1)
                if more:
                    for b in range(GB):
                        y_low(g + 1, b)

            groups(dve, body)
            for b in range(GB):
                result(NG - 1, b)

        @block.tensor
        def _(pe):
            def turn(bank, tiles):
                for n, tile in enumerate(tiles):
                    last = nc.tensor.transpose(bank[:, n * P:(n + 1) * P], tile, ident[:, :])
                return last

            def turn_x(b):
                pe.wait_ge(first_x_in[b], 16)
                after(pe, x_lo, b)
                turn(ps_t, [resid[:, b, k * P:(k + 1) * P] for k in range(KD)]).then_inc(x_turned, 1)

            def turn_y(G, b):
                after(pe, y_ready, G * GB + b + 1)
                if first(G):
                    if b == 0:
                        pe.wait_ge(b1_ready, 1)
                    after(pe, y_lo, b)
                elif b == 0:
                    if isinstance(G, int) and G <= DIRECT:
                        pe.wait_ge(tile_copied, turned_before(G, 0))
                elif b == 1:
                    if isinstance(G, int) and G <= DIRECT:
                        after(pe, e_lo, G * NC)
                    else:
                        after(pe, gelu_done, G * NC - 1)
                else:
                    after(pe, y_lo, G * GB + b - 1)
                turn(y_bank(G, b), [y[:, b, k * P:(k + 1) * P] for k in range(KD)])\
                    .then_inc(y_turned, 1)

            def turn_e(g, c):
                if c % PAIR == 0:
                    pr = c // PAIR
                    after(pe, e_in[pr % 2], experts_arrived(g, pr))
                if c == 0:
                    after(pe, y_lo, GB - 1 if first(g) else (g + 1) * GB)
                else:
                    after(pe, e_lo, g * NC + c)
                    if first(g):
                        pe.wait_ge(prep_lo, min(PREP_FIRST + c, NPREP))
                off = (c % PAIR) * P
                turn(ps_e, [e_raw[:, (c // PAIR) % 2, b, off:off + P] for b in range(GB)]).then_inc(e_turned, 1)

            def turn_prep(t):
                if t is None:
                    return
                pe.wait_ge(prep_in[t % PSLOTS], 16 * (t // PSLOTS + 1))
                if t < PREP_FIRST:
                    after(pe, prep_lo, t - 3)
                else:
                    pe.wait_ge(e_lo, t - PREP_FIRST + 1)
                turn(prep_bank(t), [prep_raw[:, t % PSLOTS, n * P:(n + 1) * P] for n in range(4)]).then_inc(prep_turned, 1)

            def turn_expert(g, c, place):
                t = turn_tile(g, c, place)
                if t is None:
                    return
                pe.wait_ge(turn_loaded[t % 2], 16 * (t // 2 + 1))
                after(pe, tile_copied, t)
                turn(ps_t, [turn_in[:, t % 2, n * P:(n + 1) * P] for n in range(4)]).then_inc(tile_turned, 1)

            def l0_slice(G, j):
                b, k = j // KD, j % KD
                if k == 0:
                    after(pe, x_lo, G * GB + b + 1)
                    after(pe, y_ready, G * GB + (b - 1 if first(G) else b))
                after(pe, w_lo, G * NC + j + 1)
                for n, (a, w) in enumerate(((0, 0), (0, 1), (1, 0))):
                    last = nc.tensor.matmul(l0_bank(G, b)[:, :], x_halves(G, b)[:, a, k, :], w_split[:, j % 2, w, :],
                                            start=(k == 0 and n == 0), stop=(k == KD - 1 and n == 2))
                last.then_inc(l0_done, 1)

            def fc1(g, c, direct):
                if c == 0:
                    after(pe, y_lo, (g + 1) * GB)
                if first(g):
                    pe.wait_ge(prep_lo, prep_count("fc1", c))
                after(pe, gelu_done, g * NC + (c if direct else c - 1))
                for k in range(KD):
                    for n, (a, w) in enumerate(((0, 0), (1, 0), (0, 1))):
                        last = nc.tensor.matmul(h_bank(c, direct)[:, :], w1[:, w, k, c * P:(c + 1) * P],
                                                y_t[:, a, k, :, :].rearrange("p b s -> p (b s)"),
                                                start=(k == 0 and n == 0), stop=(k == KD - 1 and n == 2))
                last.then_inc(fc1_done, 1)

            def fc2(g, c, within=None):
                after(pe, h_lo, g * NC + c + 1)
                after(pe, e_lo, g * NC + c + 1)
                after(pe, last_ready, g * NC + c + 1)
                if first(g) and c % 4 == 0:
                    pe.wait_ge(prep_lo, prep_count("fc2", NS - 2, c // 4))
                for b in range(GB):
                    if c == 0:
                        after(pe, out_ready, (g - 1) * GB + b + 1)
                    for n, (a, w) in enumerate(((0, 0), (0, 1), (1, 0))):
                        last = nc.tensor.matmul(ps_out[b][:, :], h[:, c % 2, a, b * S:(b + 1) * S],
                                                fc2_columns(c, c % 2, w, b),
                                                start=(c == 0 and n == 0), stop=(c == NC - 1 and n == 2))
                    last.then_inc(fc2_done, 1)
                    if b == 1 and within is not None:
                        turn_expert(*within, "within")

            pe.wait_ge(ident_ready, 1)
            for j in range(NC):
                for t in prep_beside(j):
                    if t == PSLOTS - 1:
                        turn_x(0)
                    turn_prep(t)
                l0_slice(0, j)
                if j % KD == KD - 2 and j // KD + 1 < GB:
                    turn_x(j // KD + 1)
                if j % KD == 0 and j > 0:
                    turn_y(0, j // KD - 1)
                if j == 2:
                    pe.wait_ge(consts_in, 16 * 2)
                    nc.tensor.transpose(ps_e[:, 0:NC], b1_rows, ident[0:NC, 0:NC]).then_inc(b1_turned, 1)
            turn_e(0, 0)
            turn_y(0, GB - 1)

            def body(g, more, direct):
                for c in range(NC):
                    if direct:
                        if (g, c) != (0, 0):
                            turn_e(g, c)
                        turn_expert(g, c, "before")
                    fc1(g, c, direct)
                    turn_prep(prep_in_step(g, c))
                    turn_expert(g, c, "after")
                    if more:
                        l0_slice(g + 1, c)
                    if more and c == NC - 1:
                        turn_y(g + 1, 0)
                        turn_y(g + 1, 1)
                    if c >= 1:
                        fc2(g, c - 1, within=(g, c))
                    if more and c == NC - 1:
                        turn_y(g + 1, 2)
                        turn_y(g + 1, 3)
                fc2(g, NC - 1)

            groups(pe, body)


_INS = ["x", "itok_B_0_63", "itok_B_0_15", "L0_cond_W", "L0_cond_b", "L1_cond_fc1_w", "L1_cond_fc1_b",
        "L1_cond_fc2_w", "L1_cond_fc2_b", "L1_cond_experts_w", "L1_cond_experts_b"]


def kernel(**inputs):
    import numpy as np
    import concourse.bacc as bacc
    from concourse.bass_utils import run_bass_kernel_spmd

    nc = bacc.Bacc("TRN2", target_bir_lowering=False, num_devices=1, dynamic_dma_scratch_size=DGE_SCRATCH)
    arrays, args = {}, []
    for name in _INS:
        a = np.ascontiguousarray(inputs[name])
        arrays[f"in_{name}"] = a
        args.append(nc.dram_tensor(f"in_{name}", a.shape, mybir.dt.from_np(a.dtype), kind="ExternalInput").ap())
    result = nc.dram_tensor("out_0", arrays["in_x"].shape, F32, kind="ExternalOutput").ap()
    build(nc, *args, result)
    r = run_bass_kernel_spmd(nc, [arrays], core_ids=[0])
    return r.results[0]["out_0"]
```
